# Optimizing a Trainium2 kernel written in Bass

```python
import numpy as np
import jax
import jax.numpy as jnp

def _softmax(x, axis=-1):
    return jax.nn.softmax(x, axis=axis)
def _gelu(x):
    return jax.nn.gelu(x, approximate=True)
def _silu(x):
    return jax.nn.silu(x)
def _sigmoid(x):
    return jax.nn.sigmoid(x)
def _layernorm(x, axis=-1, eps=1e-5):
    m = jnp.mean(x, axis=axis, keepdims=True)
    v = jnp.var(x, axis=axis, keepdims=True)
    return (x - m) / jnp.sqrt(v + eps)
def _scatter_add(tgt, idx, src, axis=0):
    return tgt.at[idx].add(src)
def _segment_sum(src, seg, n):
    return jax.ops.segment_sum(src, seg, n)

kernel_name = 'mk_adj_resnorm_d2_adj_256_ec004c'

def setup_inputs(seed: int = 0):
    np.random.seed(seed)
    _w = jnp.asarray
    def _rec_inputs():
        import jax
        import jax.numpy as jnp
        _gk = jax.random.key(seed)
        x = -0.0002928 + 1 * jax.random.normal(jax.random.fold_in(_gk, 1), (8, 2048, 256), jnp.float32)
        _a = jax.random.bernoulli(jax.random.fold_in(_gk, 2), 0.00390625, (8, 2048, 2048))
        _a = jnp.logical_or(_a, jnp.eye(2048, dtype=bool))
        adj = _a.astype(jnp.int32)
        return x, adj
    x, adj = _rec_inputs()
    def _L0_gnn_setup():
        import jax, jax.numpy as jnp
        import numpy as np
        NEG_INF = -9000000000000000.0
        ALPHA = 0.2
        key = jax.random.key(seed)
        k1, k2, k3, k4 = jax.random.split(key, 4)
        B, N, C_IN, C_OUT, H = (8, 2048, 256, 256, 4)
        node_feats = jax.random.normal(k1, (B, N, C_IN), dtype=jnp.float32)
        adj_matrix = jax.random.randint(k2, (B, N, N), 0, 2, dtype=jnp.int32)
        eye = jnp.eye(N, dtype=jnp.int32)[None]
        adj_matrix = jnp.maximum(adj_matrix, eye)
        W = jax.random.normal(k3, (C_OUT, C_IN), dtype=jnp.float32) * (1.414 / np.sqrt(C_IN))
        b = jnp.zeros((C_OUT,), dtype=jnp.float32)
        a = jax.random.normal(k4, (H, 2 * (C_OUT // H)), dtype=jnp.float32) * 0.1
        return {'node_feats': node_feats, 'adj_matrix': adj_matrix, 'W': W, 'b': b, 'a': a}
    _L0_gnn_all = _L0_gnn_setup()
    _L0_gnn_in = {k: v for k, v in _L0_gnn_all.items() if k in ('W', 'b', 'a', )}
    del _L0_gnn_all

    def _L1_gnn_setup():
        import jax, jax.numpy as jnp
        import numpy as np
        NEG_INF = -1000000000.0
        LRELU_ALPHA = 0.2
        key = jax.random.key(seed)
        k1, k2, k3, k4, k5 = jax.random.split(key, 5)
        B, N, Din, H, F = (8, 1024, 256, 4, 64)
        X = jax.random.normal(k1, (B, N, Din), dtype=jnp.float32)
        A = jax.random.randint(k2, (B, N, N), 0, 2).astype(jnp.int32)
        W = jax.random.normal(k3, (Din, H * F), dtype=jnp.float32) * np.sqrt(2.0 / (Din + H * F))
        a_src = jax.random.normal(k4, (H, F), dtype=jnp.float32) * np.sqrt(2.0 / (1 + F))
        a_dst = jax.random.normal(k5, (H, F), dtype=jnp.float32) * np.sqrt(2.0 / (1 + F))
        return {'X': X, 'A': A, 'W': W, 'a_src': a_src, 'a_dst': a_dst}
    _L1_gnn_all = _L1_gnn_setup()
    _L1_gnn_in = {k: v for k, v in _L1_gnn_all.items() if k in ('W', 'a_src', 'a_dst', )}
    del _L1_gnn_all

    return {
        "x": x,
        "adj": adj,
        "L0_gnn_W": _L0_gnn_in["W"],
        "L0_gnn_b": _L0_gnn_in["b"],
        "L0_gnn_a": _L0_gnn_in["a"],
        "L1_gnn_W": _L1_gnn_in["W"],
        "L1_gnn_a_src": _L1_gnn_in["a_src"],
        "L1_gnn_a_dst": _L1_gnn_in["a_dst"],
    }

def reference(x, adj, L0_gnn_W, L0_gnn_b, L0_gnn_a, L1_gnn_W, L1_gnn_a_src, L1_gnn_a_dst):
    import jax
    import jax.numpy as jnp
    def _L0_gnn_ref(node_feats, adj_matrix, W, b, a):
        import jax, jax.numpy as jnp
        import numpy as np
        NEG_INF = -9000000000000000.0
        ALPHA = 0.2
        B, N, _ = node_feats.shape
        H, two_c = a.shape
        c = two_c // 2
        f = (jnp.einsum('bni,oi->bno', node_feats, W) + b).reshape(B, N, H, c)
        a_src, a_dst = (a[:, :c], a[:, c:])
        s_src = jnp.einsum('bnhc,hc->bnh', f, a_src)
        s_dst = jnp.einsum('bnhc,hc->bnh', f, a_dst)
        logits = jax.nn.leaky_relu(s_src[:, :, None, :] + s_dst[:, None, :, :], ALPHA)
        logits = jnp.where(adj_matrix[..., None] == 1, logits, NEG_INF)
        probs = jax.nn.softmax(logits, axis=2)
        out = jnp.einsum('bijh,bjhc->bihc', probs, f)
        return out.reshape(B, N, H * c)

    def _L1_gnn_ref(X, A, W, a_src, a_dst):
        import jax, jax.numpy as jnp
        import numpy as np
        NEG_INF = -1000000000.0
        LRELU_ALPHA = 0.2
        B, N, _ = X.shape
        H, F = a_src.shape
        Wh = (X @ W).reshape(B, N, H, F)
        e_src = jnp.einsum('bnhf,hf->bnh', Wh, a_src)
        e_dst = jnp.einsum('bjhf,hf->bjh', Wh, a_dst)
        e = jax.nn.leaky_relu(e_src[:, :, None, :] + e_dst[:, None, :, :], LRELU_ALPHA)
        mask = (A > 0)[..., None]
        e = jnp.where(mask, e, NEG_INF)
        alpha = jax.nn.softmax(e, axis=2)
        Hout = jnp.einsum('bijh,bjhf->bihf', alpha, Wh)
        Hout = jax.nn.elu(Hout)
        return Hout.reshape(B, N, H * F)

    x = _layernorm(x + _L0_gnn_ref(x, adj, L0_gnn_W, L0_gnn_b, L0_gnn_a), axis=-1)
    x = _layernorm(x + _L1_gnn_ref(x, adj, L1_gnn_W, L1_gnn_a_src, L1_gnn_a_dst), axis=-1)
    return x


_drawn_inputs = setup_inputs


def setup_inputs(seed=0):
    import zlib

    import numpy as np

    out = dict(_drawn_inputs(seed))
    spreads = {'L0_gnn_b': (0.0, 0.1)}
    factors = {}
    for name, (base, spread) in spreads.items():
        noise = np.random.default_rng([zlib.crc32(name.encode()), seed]).standard_normal(out[name].shape)
        drawn = base * np.exp(spread * noise) if base else spread * noise
        out[name] = jnp.asarray(drawn.astype(out[name].dtype))
    for name, factor in factors.items():
        out[name] = (out[name] * factor).astype(out[name].dtype)
    return out
```

```python
from contextlib import ExitStack

import concourse.bass as bass
from concourse import mybir

F32 = mybir.dt.float32
F16 = mybir.dt.float16
I16 = mybir.dt.int16
I32 = mybir.dt.int32
ALU = mybir.AluOpType
ACT = mybir.ActivationFunctionType
AX = mybir.AxisListType
RMAX = bass.bass_isa.ReduceOp.max

P = 128
SLOPE = 0.2
SCALE = 2048.0
EPS = 1e-5


def gat_kernel(nc, x, adj, w0, b0, a0, w1, a1_src, a1_dst, out):
    B, N, D = x.shape
    H = a0.shape[0]
    C = D // H
    T = N // P
    K = D // P
    HALF = N // 2
    TI = HALF // P
    CE = C + 1
    R = 2 * CE
    LAYERS = 2
    UNITS = LAYERS * 2 * H
    UL = 2 * H
    STEPS = UNITS * T
    RZ, RG, RS = 4, 4, 2
    CH = 2 * TI
    GROUPS = T // 2
    PER_BANK = 512 // R
    EX = D + 2 * H
    TH = T * H

    ctx = ExitStack()
    with ctx:
        def sb(name, shape, dt=F32):
            return ctx.enter_context(nc.sbuf_tensor(name, shape, dt))

        def sem(name):
            return ctx.enter_context(nc.semaphore(name))

        stage = sb("stage", [P, RS, N // 2], I32)
        M = sb("M", [P, T, N], F16)
        X = sb("X", [P, T, D])
        F = sb("F", [P, T, H, CE])
        VF = sb("VF", [P, H * T * 4 * CE], F16)
        V = VF[:, :].rearrange("p (h t q c) -> p h t q c", h=H, t=T, q=4)
        V2 = H // 2 * T * 4 * CE
        XT = VF[:, V2:V2 + 2 * K * N].bitcast(F32)\
            .rearrange("p (k n) -> p k n", k=K)
        Z = sb("Z", [P, RZ, HALF], F16)
        G = sb("G", [P, RG, HALF], F16)
        L = sb("L", [P, RG, HALF], F16)
        sB = sb("sB", [P, 2, HALF])
        sT = sb("sT", [TH, P])
        sd = sb("sd", [P, 2, H, T])
        ss, ds = sd[:, 0, :, :], sd[:, 1, :, :]
        pm = sb("pm", [P, H])
        dmx = sb("dmx", [P, H])
        Ein = sb("Ein", [P, 4, H, T])
        E = sb("E", [P, 4, H, T])
        uu = sb("uu", [P, H, T])
        ev = sb("ev", [P, 2 * TI, 2, CE])
        c2 = sb("c2", [P, TI, CE])
        rc = sb("rc", [P, TI])
        y = sb("y", [P, TI, C])
        ye = sb("ye", [P, TI, C])
        vt = sb("vt", [P, T, CE])
        st6 = sb("st6", [P, TI, 6])
        mv = sb("mv", [P, TI, 2])
        ve = sb("ve", [P, TI])
        sq = sb("sq", [P, TI])
        rs = sb("rs", [P, TI])
        nt = sb("nt", [P, TI])
        idh = sb("idh", [P, P], F16)
        idf = sb("idf", [P, P])
        Wx = sb("Wx", [P, LAYERS, K, EX])
        amat = sb("amat", [P, LAYERS, K, 2 * H])
        bx = sb("bx", [P, LAYERS, EX])
        bcol = sb("bcol", [P, K])
        Wo = X[:, 0:LAYERS * K, :].rearrange("p (l k) c -> p l k c", l=LAYERS)
        bwide = X[:, LAYERS * K, :].rearrange("p (k n) -> p k n", k=K)

        bank = [ctx.enter_context(nc.psum_tensor(f"bank{i}", [P, 512], F32)) for i in range(6)]
        mbank = [ctx.enter_context(nc.psum_tensor(f"mbank{i}", [P, 1024], F16)) for i in range(2)]

        def acc(r):
            return bank[r // PER_BANK][:, (r % PER_BANK) * R:(r % PER_BANK + 1) * R]

        EVAC = [(b, min(PER_BANK, 2 * TI - PER_BANK * b)) for b in range(6)]

        s = {n: sem(n) for n in (
            "ident_ready w_dma wt_done wt_copied wa_done wa_copied const_ready "
            "xA_dma xB_dma out_dma stage0_dma stage1_dma mask_transposed mask_ready "
            "x_transposed xT_ready projected f_ready pmax_ready dmax_ready s_transposed sT_ready "
            "rows_dma sB0_dma sB1_dma expo_ready exp_ready factors_ready v_ready "
            "z_ready g_ready l_ready step_done evacuated ev_read c2_ready recip_ready "
            "y_ready ymin_ready yexp_ready x_updated var_ready sqrt_ready norm_ready "
            "dve_step pool_step dve_waited pool_waited").split()}
        x_dma = [s["xA_dma"], s["xB_dma"]]
        stage_dma = [s["stage0_dma"], s["stage1_dma"]]
        sB_dma = [s["sB0_dma"], s["sB1_dma"]]

        s_rows = [nc.dram_tensor(f"s_rows{l}", [H, N], F32, kind="Internal").ap() for l in range(LAYERS)]
        assert 2 * TH == P
        x_v = x.rearrange("b (t p) c -> b p t c", p=P)
        out_v = out.rearrange("b (t p) c -> b p t c", p=P)
        adj_v = adj.rearrange("b (t p) j -> b p t j", p=P)

        def unit(u):
            return u // UL, (u % UL) // H, u % H

        def mask_slot(u, j):
            l, half, h = unit(u)
            if (l, half) in ((0, 0), (1, 1)) and j % H == 1:
                return l * CH + (h * T + j) // H
            return None

        CHB = 2 * CH
        N_W = 2 * LAYERS * 2 * H + 2 * LAYERS + 1 + 1

        with nc.Block() as block:

            @block.sync
            def _(sp):
                for k in range(K):
                    sp.dma_start(Wo[:, 0, k, :], w0[k * P:(k + 1) * P, :]).then_inc(s["w_dma"], 16)
                    sp.dma_start(Wx[:, 1, k, 0:D], w1[k * P:(k + 1) * P, :]).then_inc(s["w_dma"], 16)
                    sp.dma_start(bcol[:, k:k + 1], b0[k * P:(k + 1) * P].rearrange("(p a) -> p a", a=1))\
                        .then_inc(s["w_dma"], 16)
                sp.dma_start(bx[:, 0, 0:D], b0.rearrange("(a c) -> a c", a=1).broadcast_to([P, D]))\
                    .then_inc(s["w_dma"], 16)
                sp.wait_ge(s["ident_ready"], 6)
                for l, src, dst in ((0, a0[:, 0:C], a0[:, C:2 * C]), (1, a1_src, a1_dst)):
                    for q, a in enumerate((src, dst)):
                        for h in range(H):
                            p0 = (h * C) % P
                            sp.dma_start(amat[p0:p0 + C, l, h * C // P, q * H + h:q * H + h + 1],
                                         a[h:h + 1, :].rearrange("a p -> p a")).then_inc(s["w_dma"], 16)

                def load_chunk(c, batch, c_all, first):
                    half, i, jh = (c // CH), (c % CH) // 2, c % 2
                    if not first:
                        sp.wait_ge(s["mask_transposed"], c_all - RS + 1)
                    sp.dma_start(stage[:, c % RS, :],
                                 adj_v[batch, :, half * TI + i, jh * HALF:(jh + 1) * HALF])\
                        .then_inc(stage_dma[c % RS], 16)

                for c in range(CH):
                    load_chunk(c, 0, c, c < RS)
                sp.wait_ge(s["const_ready"], 1)
                for half in range(2):
                    sp.dma_start(X[:, half * TI:(half + 1) * TI, :], x_v[0, :, half * TI:(half + 1) * TI, :])\
                        .then_inc(x_dma[half], 16)

                with sp.Fori(0, B) as b:
                    nxt = (b + 1) % B
                    for l in range(LAYERS):
                        sp.wait_ge(s["sT_ready"], b * LAYERS + l + 1)
                        sp.dma_start(s_rows[l].rearrange("h (t p) -> (h t) p", p=P), sT[:, :])\
                            .then_inc(s["rows_dma"], 16)
                        if l == 0:
                            for c in range(CH, 2 * CH):
                                load_chunk(c, b, b * CHB + c, False)
                        else:
                            for c in range(CH):
                                if c == 3 * H + 1:
                                    sp.wait_ge(s["norm_ready"], b * 4 + 3)
                                    sp.dma_start(out_v[b, :, 0:TI, :], X[:, 0:TI, :]).then_inc(s["out_dma"], 16)
                                load_chunk(c, nxt, b * CHB + CHB + c, False)
                            sp.wait_ge(s["out_dma"], b * 32 + 16)
                            sp.dma_start(X[:, 0:TI, :], x_v[nxt, :, 0:TI, :]).then_inc(x_dma[0], 16)
                    sp.wait_ge(s["norm_ready"], b * 4 + 4)
                    sp.dma_start(out_v[b, :, TI:T, :], X[:, TI:T, :]).then_inc(s["out_dma"], 16)
                    sp.wait_ge(s["out_dma"], b * 32 + 32)
                    sp.dma_start(X[:, TI:T, :], x_v[nxt, :, TI:T, :]).then_inc(x_dma[1], 16)
                for half in range(2):
                    sp.wait_ge(x_dma[half], 16 * (B + 1))
                for q in range(RS):
                    sp.wait_ge(stage_dma[q], 16 * (CH + B * CHB) // RS)

            @block.tensor
            def _(pe):
                pe.wait_ge(s["ident_ready"], 4)
                pe.wait_ge(s["w_dma"], 16 * (3 * K + 1 + LAYERS * 2 * H))
                for l in range(LAYERS):
                    src = Wo if l == 0 else Wx
                    for a in range(K):
                        for c in range(K):
                            last = pe.transpose(bank[l][:, (c * K + a) * P:(c * K + a + 1) * P],
                                                src[:, l, a, c * P:(c + 1) * P], idf[:, :])
                    last.then_inc(s["wt_done"], 1)
                pe.wait_ge(s["wt_copied"], 3)
                for l in range(LAYERS):
                    for c in range(K):
                        for o in range(K):
                            pe.matmul(bank[2][:, (l * K + c) * 8:(l * K + c) * 8 + 2 * H],
                                      Wo[:, l, o, c * P:(c + 1) * P], amat[:, l, o, :],
                                      start=o == 0, stop=o == K - 1)
                for o in range(K):
                    last = pe.matmul(bank[2][:, 64:64 + 2 * H], bwide[:, o, :], amat[:, 0, o, :],
                                     start=o == 0, stop=o == K - 1)
                last.then_inc(s["wa_done"], 1)

                def mask_chunk(c, c_all, use, first):
                    pe.wait_ge(stage_dma[c % RS], 16 * use)
                    if not first:
                        pe.wait_ge(s["mask_ready"], c_all - 1)
                    for q in range(TI):
                        last = pe.transpose(mbank[c % 2][:, q * P:(q + 1) * P],
                                            stage[:, c % RS, q * P:(q + 1) * P].bitcast(F16)[:, ::2],
                                            idh[:, :])
                    last.then_inc(s["mask_transposed"], 1)

                for c in range(CH):
                    mask_chunk(c, c, c // RS + 1, c < 2)

                with pe.Fori(0, B) as b:
                    for l in range(LAYERS):
                        pe.wait_ge(s["evacuated"], 1 + b * 3 * UNITS + 3 * UL * l)
                        for g in range(GROUPS):
                            half = g // (GROUPS // 2)
                            if g % (GROUPS // 2) == 0:
                                if l == 0:
                                    pe.wait_ge(x_dma[half], b * 16 + 16)
                                else:
                                    pe.wait_ge(s["norm_ready"], b * 4 + half + 1)
                            if g >= 2:
                                pe.wait_ge(s["xT_ready"], b * LAYERS * GROUPS + l * GROUPS + g - 1)
                            for c in range(K):
                                for t in range(2):
                                    last = pe.transpose(bank[g % 2][:, (c * 2 + t) * P:(c * 2 + t + 1) * P],
                                                        X[:, 2 * g + t, c * P:(c + 1) * P], idf[:, :])
                            last.then_inc(s["x_transposed"], 1)
                        for t in range(T):
                            pe.wait_ge(s["xT_ready"], b * LAYERS * GROUPS + l * GROUPS + t // 2 + 1)
                            if t >= 2:
                                pe.wait_ge(s["f_ready"], b * LAYERS * T + l * T + t - 1)
                            for c in range(K):
                                last = pe.matmul(bank[2 + t % 2][:, 0:EX], XT[:, c, t * P:(t + 1) * P],
                                                 Wx[:, l, c, :], start=c == 0, stop=c == K - 1)
                            last.then_inc(s["projected"], 1)
                        pe.wait_ge(s["f_ready"], b * LAYERS * T + l * T + T)
                        pe.transpose(bank[4][:, 0:P], sd[:, :, :, :].rearrange("p q h t -> p (q h t)"),
                                     idf[:, :]).then_inc(s["s_transposed"], 1)

                        for ul in range(UL):
                            u = l * UL + ul
                            _, half, h = unit(u)
                            if half == 0:
                                pe.wait_ge(s["v_ready"], b * LAYERS * H + l * H + h + 1)
                            for j in range(T):
                                k = u * T + j
                                for q, ready in enumerate(("g_ready", "l_ready")):
                                    src = (G, L)[q]
                                    pe.wait_ge(s[ready], b * STEPS + k + 1)
                                    for i in range(TI):
                                        r = q * TI + i
                                        if j == 0 and ul > 0 and r in (0, 2 * PER_BANK, 5 * PER_BANK):
                                            n = (0, 2 * PER_BANK, 5 * PER_BANK).index(r)
                                            pe.wait_ge(s["evacuated"], 1 + b * 3 * UNITS + 3 * (u - 1) + n + 1)
                                        if j == 0 and ul == 0 and r == 0:
                                            pe.wait_ge(s["sT_ready"], b * LAYERS + l + 1)
                                        last = pe.matmul(
                                            acc(r), src[:, k % RG, i * P:(i + 1) * P],
                                            V[:, h, j, 2 * q:2 * q + 2, :].rearrange("p q c -> p (q c)"),
                                            start=(j == 0 and r % PER_BANK == 0), stop=j == T - 1,
                                            skip_group_check=True)
                                last.then_inc(s["step_done"], 1)
                                c = mask_slot(u, j)
                                if c is not None:
                                    cc = CH + c
                                    mask_chunk(cc % CHB, b * CHB + cc, b * (CHB // RS) + cc // RS + 1, False)

            @block.scalar
            def _(act):
                act.sem_inc(s["evacuated"], 1)
                act.wait_ge(s["wt_done"], 1)
                act.activation(Wx[:, 0, :, 0:D], bank[0][:, :].rearrange("p (k c) -> p k c", k=K), ACT.Copy)\
                    .then_inc(s["wt_copied"], 1)
                act.wait_ge(s["wt_done"], 2)
                act.activation(Wo[:, 1, :, :], bank[1][:, :].rearrange("p (k c) -> p k c", k=K), ACT.Copy)\
                    .then_inc(s["wt_copied"], 1)

                def evacuate(bb, u):
                    act.wait_ge(s["step_done"], bb * STEPS + (u + 1) * T)
                    if u % UL > 0:
                        act.wait_ge(s["ev_read"], bb * UNITS + u)
                    for banks in ((0, 2), (2, 5), (5, 6)):
                        for n in range(*banks):
                            m = EVAC[n][1]
                            last = act.activation(
                                ev[:, n * PER_BANK:n * PER_BANK + m, :, :].rearrange("p r q c -> p (r q c)"),
                                bank[n][:, 0:m * R], ACT.Copy)
                        last.then_inc(s["evacuated"], 1)

                def spread_s(bb, u):
                    l, half, h = unit(u)
                    if u % UL == 0:
                        act.wait_ge(s["rows_dma"], 16 * (bb * LAYERS + l + 1))
                    if u % UL >= 2:
                        act.wait_ge(s["z_ready"], bb * STEPS + (u - 1) * T)
                    act.dma_start(sB[:, u % 2, :],
                                  s_rows[l][h:h + 1, half * HALF:(half + 1) * HALF].broadcast_to([P, HALF]))\
                        .then_inc(sB_dma[u % 2], 16)

                def elu_exp(bb, u):
                    act.wait_ge(s["ymin_ready"], bb * UL + u % UL + 1)
                    act.activation(ye[:, :, :], ye[:, :, :], ACT.Exp).then_inc(s["yexp_ready"], 1)

                def norm_sqrt(bb, l, half):
                    act.wait_ge(s["var_ready"], bb * 4 + l * 2 + half + 1)
                    act.activation(sq[:, :], ve[:, :], ACT.Sqrt).then_inc(s["sqrt_ready"], 1)

                with act.Fori(0, B) as b:
                    for l in range(LAYERS):
                        for g in range(GROUPS):
                            act.wait_ge(s["x_transposed"], b * LAYERS * GROUPS + l * GROUPS + g + 1)
                            act.activation(XT[:, :, 2 * g * P:2 * (g + 1) * P],
                                           bank[g % 2][:, :].rearrange("p (k n) -> p k n", k=K), ACT.Copy)\
                                .then_inc(s["xT_ready"], 1)
                        act.wait_ge(s["s_transposed"], b * LAYERS + l + 1)
                        act.activation(sT[:, :], bank[4][0:TH, 0:P], ACT.Copy).then_inc(s["sT_ready"], 1)
                        act.wait_ge(s["expo_ready"], b * LAYERS + l + 1)
                        act.activation(E[:, :, :, :], Ein[:, :, :, :], ACT.Exp).then_inc(s["exp_ready"], 1)
                        for ul in range(UL):
                            u = l * UL + ul
                            _, half, h = unit(u)
                            if ul == 0:
                                spread_s(b, u)
                            act.wait_ge(sB_dma[u % 2], 16 * (b * UNITS // 2 + u // 2 + 1))
                            for j in range(T):
                                k = u * T + j
                                if k >= RZ:
                                    act.wait_ge(s["g_ready"], b * STEPS + k - RZ + 1)
                                act.activation(Z[:, k % RZ, :], sB[:, u % 2, :], ACT.Relu,
                                               bias=ds[:, h, j:j + 1]).then_inc(s["z_ready"], 1)
                                if j == 0 and ul + 1 < UL:
                                    spread_s(b, u + 1)
                                if j == 3 and ul > 0:
                                    evacuate(b, u - 1)
                                if l == 1 and j == 7 and ul >= 2:
                                    elu_exp(b, u - 2)
                                if ul == 6 and j == 11:
                                    norm_sqrt(b, l, 0)
                        evacuate(b, u)
                        if l == 1:
                            elu_exp(b, u - 1)
                            elu_exp(b, u)
                        norm_sqrt(b, l, 1)

            @block.gpsimd
            def _(pool):
                pool.memset(idh[:, :], 0.0).then_inc(s["ident_ready"], 1)
                pool.memset(idf[:, :], 0.0).then_inc(s["ident_ready"], 1)
                pool.wait_ge(s["ident_ready"], 2)
                for m in (idh, idf):
                    pool.affine_select(out=m[:, :], in_=m[:, :], compare_op=ALU.not_equal, fill=1.0, base=0,
                                       pattern=[[-1, P]], channel_multiplier=1).then_inc(s["ident_ready"], 1)
                pool.memset(amat[:, :, :, :], 0.0).then_inc(s["ident_ready"], 1)
                pool.memset(bx[:, 1, :], 0.0).then_inc(s["ident_ready"], 1)
                pool.memset(F[:, :, :, C:CE], 1.0).then_inc(s["ident_ready"], 1)

                steps = [0]

                def link(bb, ins):
                    steps[0] += 1
                    ins.then_inc(s["pool_step"], 1)
                    pool.wait_ge(s["pool_step"], bb * POOL_STEPS + steps[0])

                def split_features(bb, l, h):
                    if h == 0:
                        pool.wait_ge(s["factors_ready"], bb * LAYERS + l + 1)
                    for q in range(2):
                        f = F[:, :, h, :]
                        e = E[:, q, h, :].unsqueeze(2).to_broadcast([P, T, CE])
                        pool.tensor_tensor(V[:, h, :, 2 * q, :], f, e, ALU.mult).then_inc(s["pool_step"], 1)
                        steps[0] += 1
                        if q == 0 and h == 1:
                            pool.wait_ge(s["v_ready"], bb * LAYERS * H + l * H + h)
                        elif q == 0 and h > 1:
                            pool.wait_ge(s["c2_ready"], bb * UNITS + l * UL + h - 1)
                        link(bb, pool.tensor_tensor(vt[:, :, :], f, e, ALU.mult))
                        last = pool.tensor_tensor(V[:, h, :, 2 * q + 1, :], vt[:, :, :], V[:, h, :, 2 * q, :],
                                                  ALU.subtract)
                        if q == 0:
                            link(bb, last)
                    last.then_inc(s["v_ready"], 1)

                def combine(bb, u):
                    l, half, h = unit(u)
                    pool.wait_ge(s["evacuated"], 1 + bb * 3 * UNITS + 3 * (u + 1))
                    if half == 0 and h + 1 < H:
                        pool.wait_ge(s["v_ready"], bb * LAYERS * H + l * H + h + 2)
                    else:
                        pool.wait_ge(s["c2_ready"], bb * UNITS + u)
                    pool.tensor_tensor(vt[:, :, :], ev[:, :, 0, :], ev[:, :, 1, :], ALU.add).then_inc(s["ev_read"], 1)
                    pool.wait_ge(s["ev_read"], bb * UNITS + u + 1)
                    link(bb, pool.tensor_tensor(
                        vt[:, :, :].rearrange("p (q i) c -> p q i c", q=2),
                        vt[:, :, :].rearrange("p (q i) c -> p q i c", q=2),
                        E[:, 2:4, h, half * TI:(half + 1) * TI].unsqueeze(3).to_broadcast([P, 2, TI, CE]),
                        ALU.mult))
                    pool.tensor_tensor(c2[:, :, :], vt[:, 0:TI, :], vt[:, TI:2 * TI, :], ALU.add)\
                        .then_inc(s["c2_ready"], 1)

                def normalise(bb, u):
                    l, half, h = unit(u)
                    pool.wait_ge(s["recip_ready"], bb * UNITS + u + 1)
                    if l == 1 and u % UL > 0:
                        pool.wait_ge(s["x_updated"], bb * UNITS + u)
                    ins = pool.tensor_tensor(y[:, :, :], c2[:, :, 0:C],
                                             rc[:, :].unsqueeze(2).to_broadcast([P, TI, C]), ALU.mult)
                    if l == 1:
                        ins.then_inc(s["y_ready"], 1)
                    else:
                        link(bb, ins)
                        xs = X[:, half * TI:(half + 1) * TI, h * C:(h + 1) * C]
                        pool.tensor_tensor(xs, xs, y[:, :, :], ALU.add).then_inc(s["x_updated"], 1)

                POOL_STEPS = LAYERS * H * 5 + UNITS + UL

                with pool.Fori(0, B) as b:
                    steps[0] = 0
                    for l in range(LAYERS):
                        pool.wait_ge(s["pmax_ready"], b * LAYERS + l + 1)
                        pool.sem_inc(s["pool_waited"], 1)
                        pool.partition_all_reduce(dmx[:, :], pm[:, :], P, RMAX).then_inc(s["dmax_ready"], 1)
                        split_features(b, l, 0)
                        for ul in range(UL):
                            u = l * UL + ul
                            _, half, h = unit(u)
                            if ul > 0:
                                combine(b, u - 1)
                            if half == 0 and h + 1 < H:
                                split_features(b, l, h + 1)
                            if ul > 0:
                                normalise(b, u - 1)
                        combine(b, u)
                        normalise(b, u)
                    assert steps[0] == POOL_STEPS, steps[0]

            @block.vector
            def _(dve):
                dve.wait_ge(s["w_dma"], 16 * (3 * K + 1 + LAYERS * 2 * H))
                dve.tensor_copy(bwide, bcol[:, :].unsqueeze(2).to_broadcast([P, K, P])).then_inc(s["wt_copied"], 1)
                dve.wait_ge(s["wa_done"], 1)
                dve.wait_ge(s["wt_copied"], 3)
                dve.wait_ge(s["ident_ready"], 7)
                dve.tensor_copy(Wx[:, :, :, D:EX].rearrange("p l k e -> p (l k) e"),
                                bank[2][:, 0:LAYERS * K * 8].rearrange("p (a e) -> p a e", e=8)[:, :, 0:2 * H])
                dve.tensor_copy(bx[:, 0, D:EX], bank[2][:, 64:64 + 2 * H]).then_inc(s["const_ready"], 1)

                def mask_copy(c, c_all):
                    half, i, jh = c // CH, (c % CH) // 2, c % 2
                    it = half * TI + i
                    dve.wait_ge(s["mask_transposed"], c_all + 1)
                    dve.tensor_copy(M[:, jh * (T // 2):(jh + 1) * (T // 2), it * P:(it + 1) * P],
                                    mbank[c % 2][:, :].bitcast(I16).rearrange("p (q n) -> p q n", n=P))\
                        .then_inc(s["mask_ready"], 1)

                for c in range(CH):
                    mask_copy(c, c)

                steps = [0]

                def link(bb, ins):
                    steps[0] += 1
                    ins.then_inc(s["dve_step"], 1)
                    dve.wait_ge(s["dve_step"], bb * DVE_STEPS + steps[0])

                def reciprocal(bb, u):
                    dve.wait_ge(s["c2_ready"], bb * UNITS + u + 1)
                    dve.reciprocal(rc[:, :], c2[:, :, C]).then_inc(s["recip_ready"], 1)

                def elu_min(bb, u):
                    dve.wait_ge(s["y_ready"], bb * UL + u % UL + 1)
                    dve.tensor_scalar(ye[:, :, :], y[:, :, :], 0.0, None, ALU.min).then_inc(s["ymin_ready"], 1)

                def elu_add(bb, u):
                    _, half, h = unit(u)
                    dve.wait_ge(s["yexp_ready"], bb * UL + u % UL + 1)
                    link(bb, dve.scalar_tensor_tensor(y[:, :, :], y[:, :, :], 0.0, ye[:, :, :], ALU.max, ALU.add))
                    xs = X[:, half * TI:(half + 1) * TI, h * C:(h + 1) * C]
                    dve.scalar_tensor_tensor(xs, y[:, :, :], -1.0, xs, ALU.add, ALU.add).then_inc(s["x_updated"], 1)

                def stats(bb, l, half, i):
                    if i == 0:
                        dve.wait_ge(s["x_updated"], bb * UNITS + l * UL + half * H + H)
                    dve.bn_stats(st6[:, i, :], X[:, half * TI + i, :]).then_inc(s["dve_step"], 1)
                    steps[0] += 1

                def variance(bb):
                    dve.wait_ge(s["dve_step"], bb * DVE_STEPS + steps[0])
                    dve.sem_inc(s["dve_waited"], 1)
                    for i in range(TI):
                        last = dve.bn_aggr(mv[:, i, :], st6[:, i, :])
                    link(bb, last)
                    dve.tensor_scalar(ve[:, :], mv[:, :, 1], EPS, None, ALU.add).then_inc(s["var_ready"], 1)

                def layer_norm(bb, l, half):
                    dve.wait_ge(s["sqrt_ready"], bb * 4 + l * 2 + half + 1)
                    link(bb, dve.reciprocal(rs[:, :], sq[:, :]))
                    link(bb, dve.tensor_tensor(nt[:, :], rs[:, :], rs[:, :], ALU.mult))
                    link(bb, dve.tensor_tensor(nt[:, :], nt[:, :], ve[:, :], ALU.mult))
                    link(bb, dve.tensor_scalar(nt[:, :], nt[:, :], -0.5, 1.5, ALU.mult, ALU.add))
                    link(bb, dve.tensor_tensor(rs[:, :], rs[:, :], nt[:, :], ALU.mult))
                    for i in range(TI):
                        xi = X[:, half * TI + i, :]
                        last = dve.tensor_scalar(xi, xi, mv[:, i, 0:1], rs[:, i:i + 1], ALU.subtract, ALU.mult)
                    last.then_inc(s["norm_ready"], 1)

                DVE_STEPS = LAYERS * (1 + 2 * (TI + 1 + 5)) + UL

                with dve.Fori(0, B) as b:
                    steps[0] = 0
                    for l in range(LAYERS):
                        for t in range(T):
                            dve.wait_ge(s["projected"], b * LAYERS * T + l * T + t + 1)
                            pb = bank[2 + t % 2]
                            dve.tensor_tensor(F[:, t, :, 0:C], pb[:, 0:D].rearrange("p (h c) -> p h c", h=H),
                                              bx[:, l, 0:D].rearrange("p (h c) -> p h c", h=H), ALU.add)
                            dve.tensor_tensor(ss[:, :, t], pb[:, D:D + H], bx[:, l, D:D + H], ALU.add)
                            dve.tensor_tensor(ds[:, :, t], pb[:, D + H:EX], bx[:, l, D + H:EX], ALU.add)\
                                .then_inc(s["f_ready"], 1)
                        dve.wait_ge(s["f_ready"], b * LAYERS * T + l * T + T)
                        dve.tensor_reduce(pm[:, :], ds[:, :, :], AX.X, ALU.max).then_inc(s["pmax_ready"], 1)
                        dve.wait_ge(s["dmax_ready"], b * LAYERS + l + 1)
                        dm = dmx[:, :].unsqueeze(2).to_broadcast([P, H, T])
                        dve.tensor_tensor(Ein[:, 0, :, :], ds[:, :, :], dm, ALU.subtract)
                        link(b, dve.tensor_tensor(uu[:, :, :], ss[:, :, :], dm, ALU.add))
                        dve.tensor_scalar(Ein[:, 1, :, :], Ein[:, 0, :, :], SLOPE, None, ALU.mult)
                        dve.tensor_scalar(Ein[:, 2, :, :], uu[:, :, :], 1.0 - SLOPE, 0.0, ALU.mult, ALU.min)
                        dve.tensor_scalar(Ein[:, 3, :, :], uu[:, :, :], SLOPE - 1.0, 0.0, ALU.mult, ALU.min)\
                            .then_inc(s["expo_ready"], 1)
                        dve.wait_ge(s["exp_ready"], b * LAYERS + l + 1)
                        dve.tensor_scalar(E[:, 0:2, :, :], E[:, 0:2, :, :], SCALE, None, ALU.mult)\
                            .then_inc(s["factors_ready"], 1)

                        def lower(k, u, j):
                            half = unit(u)[1]
                            dve.wait_ge(s["g_ready"], b * STEPS + k + 1)
                            dve.tensor_tensor(L[:, k % RG, :], M[:, j, half * HALF:(half + 1) * HALF],
                                              G[:, k % RG, :], ALU.subtract).then_inc(s["l_ready"], 1)

                        for ul in range(UL):
                            u = l * UL + ul
                            _, half, h = unit(u)
                            if h == 0:
                                dve.wait_ge(s["mask_ready"], b * CHB + (CH if half == 0 else 2 * CH))
                            for j in range(T):
                                k = u * T + j
                                dve.wait_ge(s["z_ready"], b * STEPS + k + 1)
                                if k >= RG:
                                    dve.wait_ge(s["step_done"], b * STEPS + k - RG + 1)
                                dve.tensor_tensor(G[:, k % RG, :], Z[:, k % RZ, :],
                                                  M[:, j, half * HALF:(half + 1) * HALF], ALU.logical_and)\
                                    .then_inc(s["g_ready"], 1)
                                if j > 0:
                                    lower(k - 1, u, j - 1)
                                if ul > 0 and j == 9:
                                    reciprocal(b, u - 1)
                                if l == 1 and ul >= 2 and j == 5:
                                    elu_min(b, u - 2)
                                if l == 1 and ul >= 2 and j == 10:
                                    elu_add(b, u - 2)
                                if ul == 6 and 1 <= j <= TI and l == 0:
                                    stats(b, l, 0, j - 1)
                                if ul == 6 and j == 10:
                                    if l == 1:
                                        for i in range(TI):
                                            stats(b, l, 0, i)
                                    variance(b)
                                if ul == 6 and j == 14:
                                    layer_norm(b, l, 0)
                                if j >= 3:
                                    c = mask_slot(u, j - 2)
                                    if c is not None:
                                        cc = CH + c
                                        mask_copy(cc % CHB, b * CHB + cc)
                            lower(k, u, j)
                        if l == 1:
                            elu_min(b, u - 1)
                            elu_add(b, u - 1)
                        reciprocal(b, u)
                        if l == 1:
                            elu_min(b, u)
                            elu_add(b, u)
                        for i in range(TI):
                            stats(b, l, 1, i)
                        variance(b)
                        layer_norm(b, l, 1)
                    assert steps[0] == DVE_STEPS, steps[0]


_INS = ["x", "adj", "L0_gnn_W", "L0_gnn_b", "L0_gnn_a", "L1_gnn_W", "L1_gnn_a_src", "L1_gnn_a_dst"]


def kernel(**inputs):
    import numpy as _np
    import concourse.bacc as _bacc
    from concourse import mybir as _mybir
    from concourse.bass_utils import run_bass_kernel_spmd as _run

    nc = _bacc.Bacc("TRN2", target_bir_lowering=False, num_devices=1)
    arrays, args = {}, []
    for name in _INS:
        a = _np.ascontiguousarray(inputs[name])
        arrays[f"in_{name}_dram"] = a
        args.append(nc.dram_tensor(f"in_{name}_dram", a.shape, _mybir.dt.from_np(a.dtype), kind="ExternalInput").ap())
    out = nc.dram_tensor("out_0_dram", inputs["x"].shape, _mybir.dt.float32, kind="ExternalOutput").ap()
    gat_kernel(nc, *args, out)
    r = _run(nc, [arrays], core_ids=[0])
    return r.results[0]["out_0_dram"]
```

```python
from contextlib import ExitStack

import concourse.bass as bass
from concourse import mybir

F32 = mybir.dt.float32
F16 = mybir.dt.float16
I16 = mybir.dt.int16
I32 = mybir.dt.int32
ALU = mybir.AluOpType
ACT = mybir.ActivationFunctionType
AX = mybir.AxisListType
RMAX = bass.bass_isa.ReduceOp.max

P = 128
SLOPE = 0.2
SCALE = 2048.0
EPS = 1e-5


def gat_kernel(nc, x, adj, w0, b0, a0, w1, a1_src, a1_dst, out):
    B, N, D = x.shape
    H = a0.shape[0]
    C = D // H
    T = N // P
    K = D // P
    HALF = N // 2
    TI = HALF // P
    CE = C + 1
    R = 2 * CE
    LAYERS = 2
    WARM_UP = 50
    UL = 2 * H
    UNITS = LAYERS * UL
    TP = T // 2
    PAIRS = UNITS * TP
    RING = 6
    LAG = 2
    RS = 2
    CH = 2 * TI
    CHB = 2 * CH
    GROUPS = T // 2
    PER_BANK = 512 // R
    EX = D + 2 * H
    EARLY = H

    ctx = ExitStack()
    with ctx:
        def sb(name, shape, dt=F32):
            return ctx.enter_context(nc.sbuf_tensor(name, shape, dt))

        def sem(name):
            return ctx.enter_context(nc.semaphore(name))

        stage = sb("stage", [P, RS, N // 2], I32)
        M = sb("M", [P, T, N], F16)
        X = sb("X", [P, T, D])
        xin = sb("xin", [P, 2, 2, D])
        XT = sb("XT", [P, 2, K, 2 * P])
        F = sb("F", [P, T, H, CE])
        V = sb("V", [P, H, T, 4, CE], F16)
        GL = sb("GL", [P, 2 * RING, HALF], F16)
        sB = sb("sB", [P, 2, HALF])
        sT = sb("sT", [H * T, P])
        sd = sb("sd", [P, LAYERS, 2, H, T])
        pm = sb("pm", [P, H])
        dmx = sb("dmx", [P, H])
        Ein = sb("Ein", [P, 4, H, T])
        E = sb("E", [P, LAYERS, 4, H, T])
        uu = sb("uu", [P, H, T])
        ev = sb("ev", [P, 2 * TI, 2, CE])
        vt = sb("vt", [P, T, CE])
        c2 = sb("c2", [P, TI, CE])
        rc = sb("rc", [P, TI])
        y = sb("y", [P, TI, C])
        ye = sb("ye", [P, TI, C])
        st6 = sb("st6", [P, TI, 6])
        mv = sb("mv", [P, TI, 2])
        ve = sb("ve", [P, TI])
        sq = sb("sq", [P, TI])
        rs = sb("rs", [P, TI])
        nt = sb("nt", [P, TI])
        idh = sb("idh", [P, P], F16)
        idf = sb("idf", [P, P])
        Wx = sb("Wx", [P, LAYERS, K, EX])
        amat = sb("amat", [P, LAYERS, K, 2 * H])
        bx = sb("bx", [P, LAYERS, EX])
        bcol = sb("bcol", [P, K])
        Wo = X[:, 0:LAYERS * K, :].rearrange("p (l k) c -> p l k c", l=LAYERS)
        bwide = X[:, LAYERS * K, :].rearrange("p (k n) -> p k n", k=K)
        v0t = ev[:, :, :, :].rearrange("p r q c -> p (r q c)")[:, 0:T * CE]\
            .rearrange("p (t c) -> p t c", c=CE)

        bank = [ctx.enter_context(nc.psum_tensor(f"bank{i}", [P, 512], F32)) for i in range(8)]

        def acc(r):
            return bank[r // PER_BANK][:, (r % PER_BANK) * R:(r % PER_BANK + 1) * R]

        EVAC = [(i, i + 1) for i in range(-(-2 * TI // PER_BANK))]

        PARTS = len(EVAC)

        s = {n: sem(n) for n in (
            "ident_ready w_dma wt_done wt_copied wa_done const_ready "
            "xA_dma xB_dma out_dma stage0_dma stage1_dma xin0_dma xin1_dma mask_transposed mask_ready "
            "x_transposed xT_ready tiles_normed projected f_ready pmax_ready dmax_ready s_transposed sT_ready "
            "rows_dma sB0_dma sB1_dma expo_ready exp_ready factors_ready v_ready v0_ready "
            "z_ready g_ready g_used l_ready pair_done evacuated ev_read c2_ready recip_ready "
            "rs_ready y_ready yneg_ready yexp_ready x_updated var_ready sqrt_ready norm_ready "
            "dve_step pool_step dve_waited pool_waited").split()}
        x_dma = [s["xA_dma"], s["xB_dma"]]
        stage_dma = [s["stage0_dma"], s["stage1_dma"]]
        sB_dma = [s["sB0_dma"], s["sB1_dma"]]
        xin_dma = [s["xin0_dma"], s["xin1_dma"]]

        s_rows = [nc.dram_tensor(f"s_rows{l}", [H, N], F32, kind="Internal").ap() for l in range(LAYERS)]
        assert 2 * H * T == P
        x_v = x.rearrange("b (t p) c -> b p t c", p=P)
        out_v = out.rearrange("b (t p) c -> b p t c", p=P)
        adj_v = adj.rearrange("b (t p) j -> b p t j", p=P)

        def unit(u):
            return u // UL, (u % UL) // H, u % H

        def first(v):
            return isinstance(v, int) and v <= 0

        short = next(n for n in range(RING) if (PAIRS - n * (RING - 1)) % RING == 0)
        full = (PAIRS - short * (RING - 1)) // RING
        before = 4
        SLOT = [i for n in range(full + short)
                for i in range(RING - 1 if before <= n < before + short else RING)]
        assert len(SLOT) == PAIRS

        def slot_before(pair):
            return next(q for q in range(pair - 1, pair - PAIRS, -1) if SLOT[q % PAIRS] == SLOT[pair])

        PAIR_STEPS = [[("G", p)] + ([("L", p - LAG)] if p >= LAG else []) for p in range(TP)]
        PAIR_STEPS[-1] += [("L", p) for p in range(TP - LAG, TP)]

        MASK_AT = {(c // H, 3 * (c % H) + 4): CH + c for c in range(CH)}
        MASK_AT |= {(UNITS - H + c // H, 3 * (c % H) + 4): c for c in range(CH)}
        PREP1_AT = {}
        PREP0_AT = {}
        for at, k0, groups, period in ((PREP1_AT, (UL - 2) * T + 2, GROUPS // 2, 5),
                                       (PREP0_AT, (UNITS - 6) * T + 8, GROUPS, 7)):
            for g in range(groups):
                k = k0 + period * g
                at[k] = ("T", g)
                at[k + period + 3], at[k + period + 4] = ("P", 2 * g), ("P", 2 * g + 1)
            at[k + period + 6] = ("S", 0)
        S1_AT = max(PREP1_AT)
        ROWS0_AT = (UNITS - 1) * T - 2
        ROWS1_AT = UL * T - 2
        ROW_DMAS = 1 + 2 * H
        EARLY_G = 3
        ACT_LAG = 8
        EVAC_AT = 6
        JOB_BANK, order = {}, []
        for k in range(UNITS * T):
            u, j = k // T, k % T
            if (u, j) in MASK_AT:
                order.append((k, "M", MASK_AT[u, j]))
            for at in (PREP1_AT, PREP0_AT):
                if k in at:
                    order.append((k, *at[k]))
        for n, (k, kind, m) in enumerate(order):
            JOB_BANK[k, kind, m] = (6 + n % 2, order[n - 2][1:] + (order[n - 2][0],) if n >= 2 else None)

        def prep_plan(k):
            if k in PREP1_AT:
                return 1, PREP1_AT[k]
            if k in PREP0_AT:
                return 0, PREP0_AT[k]
            return None

        with nc.Block() as block:

            @block.sync
            def _(sp):
                for k in range(K):
                    sp.dma_start(Wo[:, 0, k, :], w0[k * P:(k + 1) * P, :]).then_inc(s["w_dma"], 16)
                    sp.dma_start(Wx[:, 1, k, 0:D], w1[k * P:(k + 1) * P, :]).then_inc(s["w_dma"], 16)
                    sp.dma_start(bcol[:, k:k + 1], b0[k * P:(k + 1) * P].rearrange("(p a) -> p a", a=1))\
                        .then_inc(s["w_dma"], 16)
                sp.dma_start(bx[:, 0, 0:D], b0.rearrange("(a c) -> a c", a=1).broadcast_to([P, D]))\
                    .then_inc(s["w_dma"], 16)
                sp.wait_ge(s["ident_ready"], 6)
                for l, src, dst in ((0, a0[:, 0:C], a0[:, C:2 * C]), (1, a1_src, a1_dst)):
                    for q, a in enumerate((src, dst)):
                        for h in range(H):
                            p0 = (h * C) % P
                            sp.dma_start(amat[p0:p0 + C, l, h * C // P, q * H + h:q * H + h + 1],
                                         a[h:h + 1, :].rearrange("a p -> p a")).then_inc(s["w_dma"], 16)

                def load_chunk(c, batch, c_all):
                    half, i, jh = (c // CH), (c % CH) // 2, c % 2
                    if not first(c_all - RS + 1):
                        sp.wait_ge(s["mask_transposed"], c_all - RS + 1)
                    sp.dma_start(stage[:, c % RS, :],
                                 adj_v[batch, :, half * TI + i, jh * HALF:(jh + 1) * HALF])\
                        .then_inc(stage_dma[c % RS], 16)

                def load_group(g, batch):
                    if not first(batch * LAYERS * GROUPS + g - 1):
                        sp.wait_ge(s["x_transposed"], batch * LAYERS * GROUPS + max(g - 1, 0))
                    sp.dma_start(xin[:, g % 2, :, :], x_v[batch, :, 2 * g:2 * g + 2, :]).then_inc(xin_dma[g % 2], 16)

                def rows0(b):
                    sp.wait_ge(s["sT_ready"], 3 * b + 1)
                    sp.dma_start(s_rows[0].rearrange("h (t p) -> (h t) p", p=P), sT[:, :])\
                        .then_inc(s["rows_dma"], 16)

                def rows1(b, half):
                    sp.wait_ge(s["sT_ready"], 3 * b + 2 + half)
                    for h in range(H):
                        sp.dma_start(s_rows[1][h, half * HALF:(half + 1) * HALF].rearrange("(t p) -> t p", p=P),
                                     sT[h * T + half * TI:h * T + (half + 1) * TI, :]).then_inc(s["rows_dma"], 16)

                for g in range(GROUPS):
                    load_group(g, 0)
                for c in range(CH):
                    load_chunk(c, 0, c)
                sp.wait_ge(s["const_ready"], 1)
                for half in range(2):
                    sp.dma_start(X[:, half * TI:(half + 1) * TI, :], x_v[0, :, half * TI:(half + 1) * TI, :])\
                        .then_inc(x_dma[half], 16)
                rows0(0)

                def loads(b, units, nxt, prev=None):
                    for k in range(units[0] * T, units[-1] * T + T):
                        u, j = k // T, k % T
                        c = MASK_AT.get((u, j))
                        if c is not None and c >= CH:
                            load_chunk(c, b, b * CHB + c)
                        elif c is not None and nxt is not None:
                            load_chunk(c, nxt, nxt * CHB + c)
                        if k in PREP0_AT and nxt is not None:
                            kind, g = PREP0_AT[k]
                            if kind == "T":
                                load_group(g, nxt)
                        if k == ROWS0_AT and nxt is not None:
                            rows0(nxt)
                        if k == (UNITS - 1) * T + 15:
                            sp.wait_ge(s["norm_ready"], b * 3 + 2)
                            sp.dma_start(out_v[b, :, 0:TI, :], X[:, 0:TI, :]).then_inc(s["out_dma"], 16)
                        if k == T // 2 and prev is not None:
                            sp.wait_ge(s["out_dma"], prev * 32 + 16)
                            sp.dma_start(X[:, 0:TI, :], x_v[b, :, 0:TI, :]).then_inc(x_dma[0], 16)
                        if k in (ROWS1_AT, UL * T):
                            rows1(b, int(k == UL * T))

                loads(0, range(0, EARLY), 1)
                if B > 1:
                    with sp.Fori(0, B - 1) as b:
                        loads(b, range(EARLY, UNITS), b + 1)
                        loads(b + 1, range(0, EARLY), None, b)
                        sp.wait_ge(s["norm_ready"], b * 3 + 3)
                        sp.dma_start(out_v[b, :, TI:T, :], X[:, TI:T, :]).then_inc(s["out_dma"], 16)
                        sp.wait_ge(s["out_dma"], b * 32 + 32)
                        sp.dma_start(X[:, TI:T, :], x_v[b + 1, :, TI:T, :]).then_inc(x_dma[1], 16)
                loads(B - 1, range(EARLY, UNITS), None)

            @block.tensor
            def _(pe):
                pe.wait_ge(s["ident_ready"], 4)
                pe.wait_ge(s["w_dma"], 16 * (3 * K + 1 + LAYERS * 2 * H))
                for l in range(LAYERS):
                    src = Wo if l == 0 else Wx
                    for a in range(K):
                        for c in range(K):
                            last = pe.transpose(bank[l][:, (c * K + a) * P:(c * K + a + 1) * P],
                                                src[:, l, a, c * P:(c + 1) * P], idf[:, :])
                    last.then_inc(s["wt_done"], 1)
                pe.wait_ge(s["wt_copied"], 3)
                for l in range(LAYERS):
                    for c in range(K):
                        for o in range(K):
                            pe.matmul(bank[2][:, (l * K + c) * 8:(l * K + c) * 8 + 2 * H],
                                      Wo[:, l, o, c * P:(c + 1) * P], amat[:, l, o, :],
                                      start=o == 0, stop=o == K - 1)
                for o in range(K):
                    last = pe.matmul(bank[2][:, 64:64 + 2 * H], bwide[:, o, :], amat[:, 0, o, :],
                                     start=o == 0, stop=o == K - 1)
                last.then_inc(s["wa_done"], 1)

                def mask_chunk(c, c_all, bk, use):
                    pe.wait_ge(stage_dma[c % RS], 16 * use)
                    for q in range(TI):
                        last = pe.transpose(bank[bk][:, q * P // 2:(q + 1) * P // 2].bitcast(F16),
                                            stage[:, c % RS, q * P:(q + 1) * P].bitcast(F16)[:, ::2],
                                            idh[:, :])
                    last.then_inc(s["mask_transposed"], 1)

                def transpose_group(n, l, g, bk):
                    for c in range(K):
                        for t in range(2):
                            src = xin[:, g % 2, t, :] if l == 0 else X[:, 2 * g + t, :]
                            last = pe.transpose(bank[bk][:, (c * 2 + t) * P:(c * 2 + t + 1) * P],
                                                src[:, c * P:(c + 1) * P], idf[:, :])
                    last.then_inc(s["x_transposed"], 1)

                def project(n, l, t, bk):
                    pe.wait_ge(s["xT_ready"], n * GROUPS + t // 2 + 1)
                    for c in range(K):
                        last = pe.matmul(bank[bk][:, 0:EX], XT[:, t // 2 % 2, c, t % 2 * P:(t % 2 + 1) * P],
                                         Wx[:, l, c, :], start=c == 0, stop=c == K - 1)
                    last.then_inc(s["projected"], 1)

                def transpose_s(n, l, bk, tiles=T):
                    pe.wait_ge(s["f_ready"], n * T + tiles)
                    pe.transpose(bank[bk][:, 0:P], sd[:, l, :, :, :].rearrange("p q h t -> p (q h t)"),
                                 idf[:, :]).then_inc(s["s_transposed"], 1)

                def prepare_at_once(b, l, groups):
                    first_group = groups[0]
                    n = b * LAYERS + l

                    def transposed(g):
                        if l == 0:
                            pe.wait_ge(xin_dma[g % 2], 16 * (g // 2 + 1))
                        else:
                            pe.wait_ge(s["tiles_normed"], b * (GROUPS // 2) + g - first_group + 1)
                        if g - first_group >= 2:
                            pe.wait_ge(s["xT_ready"], n * GROUPS + g - 1)
                        transpose_group(n, l, g, g % 2)

                    transposed(groups[0])
                    for g in groups:
                        if g + 1 in groups:
                            transposed(g + 1)
                        for t in (2 * g, 2 * g + 1):
                            if t - 2 * first_group >= 2:
                                pe.wait_ge(s["f_ready"], n * T + t - 1)
                            project(n, l, t, 2 + t % 2)
                    transpose_s(n, l, 4)

                pe.wait_ge(s["const_ready"], 1)
                prepare_at_once(0, 0, range(GROUPS))
                for c in range(CH):
                    if c >= 2:
                        pe.wait_ge(s["mask_ready"], c - 1)
                    mask_chunk(c, c, 6 + c % 2, c // RS + 1)

                def bank_free(b, nxt, job):
                    kind, m, k = job
                    if kind == "M":
                        pe.wait_ge(s["mask_ready"], (b if m >= CH else nxt) * CHB + m + 1)
                        return
                    n = b * LAYERS + 1 if k in PREP1_AT else nxt * LAYERS
                    if kind == "T":
                        pe.wait_ge(s["xT_ready"], n * GROUPS + m + 1)
                    elif kind == "P":
                        pe.wait_ge(s["f_ready"], n * T + m + 1)
                    else:
                        pe.wait_ge(s["sT_ready"], 3 * b + 2 if k in PREP1_AT else 3 * nxt + 1)

                def side_jobs(b, nxt, k):
                    u, j = k // T, k % T
                    c = MASK_AT.get((u, j))
                    if c is not None and (c >= CH or nxt is not None):
                        bk, before = JOB_BANK[k, "M", c]
                        if before:
                            bank_free(b, nxt, before)
                        c_all = (b if c >= CH else nxt) * CHB + c
                        mask_chunk(c, c_all, bk, (b if c >= CH else nxt) * (CHB // RS) + c // RS + 1)
                    prep = prep_plan(k)
                    if prep is None or (prep[0] == 0 and nxt is None):
                        return
                    l, (kind, m) = prep
                    n = b * LAYERS + 1 if l else nxt * LAYERS
                    bk, before = JOB_BANK[k, kind, m]
                    if before and (before[0] != "M" or before[1] >= CH or nxt is not None):
                        bank_free(b, nxt, before)
                    if kind == "T":
                        if l == 0:
                            pe.wait_ge(xin_dma[m % 2], 16 * (nxt * (GROUPS // 2) + m // 2 + 1))
                        elif m == 0:
                            pe.wait_ge(s["norm_ready"], b * 3 + 1)
                        transpose_group(n, l, m, bk)
                    elif kind == "P":
                        project(n, l, m, bk)
                    else:
                        transpose_s(n, l, bk, TI if l else T)

                def work(b, units, nxt):
                    for u in units:
                        l, half, h = unit(u)
                        n = b * LAYERS + l
                        if u == UL:
                            pe.wait_ge(s["evacuated"], PARTS * (b * UNITS + u))
                            pe.wait_ge(s["x_updated"], b * UNITS + UL)
                            for _ in range(WARM_UP):
                                pe.matmul(bank[5][:, 0:P], idh[:, :], idh[:, :], start=True, stop=True)
                            prepare_at_once(b, 1, range(GROUPS // 2, GROUPS))
                            pe.wait_ge(s["sT_ready"], 3 * b + 3)
                            pe.wait_ge(s["v0_ready"], b + 1)
                        if half == 0 and u != UL:
                            pe.wait_ge(s["v_ready"], n * H + h + 1)
                        for jp in range(TP):
                            for kind, p in PAIR_STEPS[jp]:
                                q = "GL".index(kind)
                                pair = u * TP + p
                                if u == UL and (kind, p) == ("L", 0):
                                    pe.wait_ge(s["v_ready"], n * H + 1)
                                pe.wait_ge(s["l_ready" if q else "g_ready"], b * PAIRS + pair + 1)
                                for j in (2 * p, 2 * p + 1):
                                    for i in range(TI):
                                        r = q * TI + i
                                        for n_ev, (b0_, _) in enumerate(EVAC):
                                            if j == 0 and r == b0_ * PER_BANK and not first(b * UNITS + u):
                                                pe.wait_ge(s["evacuated"], PARTS * (b * UNITS + u - 1) + n_ev + 1)
                                        last = pe.matmul(
                                            acc(r), GL[:, SLOT[pair] * 2 + j % 2, i * P:(i + 1) * P],
                                            V[:, h, j, 2 * q:2 * q + 2, :].rearrange("p q c -> p (q c)"),
                                            start=(j == 0 and r % PER_BANK == 0), stop=j == T - 1,
                                            skip_group_check=True)
                                last.then_inc(s["pair_done" if q else "g_used"], 1)
                            for jj in range(2):
                                side_jobs(b, nxt, u * T + 2 * jp + jj)

                pe.wait_ge(s["sT_ready"], 1)
                work(0, range(0, EARLY), 1)
                if B > 1:
                    with pe.Fori(0, B - 1) as b:
                        work(b, range(EARLY, UNITS), b + 1)
                        work(b + 1, range(0, EARLY), b + 2)
                work(B - 1, range(EARLY, UNITS), None)

            @block.scalar
            def _(act):
                act.wait_ge(s["wt_done"], 1)
                act.activation(Wx[:, 0, :, 0:D], bank[0][:, :].rearrange("p (k c) -> p k c", k=K), ACT.Copy)\
                    .then_inc(s["wt_copied"], 1)
                act.wait_ge(s["wt_done"], 2)
                act.activation(Wo[:, 1, :, :], bank[1][:, :].rearrange("p (k c) -> p k c", k=K), ACT.Copy)\
                    .then_inc(s["wt_copied"], 1)

                def copy_xT(n, g, bk):
                    act.wait_ge(s["x_transposed"], n * GROUPS + g + 1)
                    if g >= 2:
                        act.wait_ge(s["projected"], n * T + 2 * (g - 1))
                    act.activation(XT[:, g % 2, :, :], bank[bk][:, :].rearrange("p (k n) -> p k n", k=K),
                                   ACT.Copy).then_inc(s["xT_ready"], 1)

                def copy_sT(count, bk):
                    act.wait_ge(s["s_transposed"], count)
                    act.activation(sT[:, :], bank[bk][0:H * T, 0:P], ACT.Copy).then_inc(s["sT_ready"], 1)

                def factors(n, l):
                    act.wait_ge(s["expo_ready"], n + 1)
                    act.activation(E[:, l, :, :, :], Ein[:, :, :, :], ACT.Exp).then_inc(s["exp_ready"], 1)

                def spread_s(b, u):
                    l, half, h = unit(u)
                    if h == 0 and (l, half) != (0, 1):
                        act.wait_ge(s["rows_dma"], 16 * (b * ROW_DMAS + 1 + l * (half + 1) * H))
                    if not first(b * UNITS + u - 1):
                        act.wait_ge(s["z_ready"], (b * UNITS + u - 1) * TP)
                    act.dma_start(sB[:, u % 2, :],
                                  s_rows[l][h:h + 1, half * HALF:(half + 1) * HALF].broadcast_to([P, HALF]))\
                        .then_inc(sB_dma[u % 2], 16)

                def evacuate(b, u):
                    act.wait_ge(s["pair_done"], (b * UNITS + u + 1) * TP)
                    if not first(b * UNITS + u):
                        act.wait_ge(s["ev_read"], b * UNITS + u)
                    if u == UL:
                        act.wait_ge(s["v0_ready"], b + 1)
                    for banks in EVAC:
                        for i in range(*banks):
                            m = min(PER_BANK, 2 * TI - PER_BANK * i)
                            last = act.activation(
                                ev[:, i * PER_BANK:i * PER_BANK + m, :, :].rearrange("p r q c -> p (r q c)"),
                                bank[i][:, 0:m * R], ACT.Copy)
                        last.then_inc(s["evacuated"], 1)

                def elu_exp(b, u):
                    count = b * UL + u % UL + 1
                    act.wait_ge(s["y_ready"], count)
                    act.activation(ye[:, :, :], y[:, :, :], ACT.Relu, scale=-1.0).then_inc(s["yneg_ready"], 1)
                    act.wait_ge(s["yneg_ready"], count)
                    act.activation(ye[:, :, :], ye[:, :, :], ACT.Exp, scale=-1.0).then_inc(s["yexp_ready"], 1)

                def norm_sqrt(b, l, half):
                    act.wait_ge(s["var_ready"], b * 4 + l * 2 + half + 1)
                    act.activation(sq[:, :], ve[:, :], ACT.Sqrt).then_inc(s["sqrt_ready"], 1)

                def normalise_rows(b, half):
                    act.wait_ge(s["rs_ready"], b * 2 + half + 1)
                    for i in range(TI):
                        xi = X[:, half * TI + i, :]
                        last = act.activation(xi, xi, ACT.Identity, bias=nt[:, i:i + 1], scale=rs[:, i:i + 1])
                    last.then_inc(s["norm_ready"], 1)

                def store(b, half):
                    act.wait_ge(s["norm_ready"], b * 3 + half + 2)
                    act.dma_start(out_v[b, :, half * TI:(half + 1) * TI, :], X[:, half * TI:(half + 1) * TI, :])\
                        .then_inc(s["out_dma"], 16)

                for g in range(GROUPS):
                    copy_xT(0, g, g % 2)
                copy_sT(1, 4)
                factors(0, 0)
                spread_s(0, 0)

                def work(b, units, nxt, prev):
                    for u in units:
                        l, half, h = unit(u)
                        ul = u % UL
                        if u == UL:
                            copy_sT(3 * b + 2, JOB_BANK[S1_AT, "S", 0][0])
                            spread_s(b, u)
                            evacuate(b, u - 1)
                        act.wait_ge(sB_dma[u % 2], 16 * (b * (UNITS // 2) + u // 2 + 1))
                        for j in range(T):
                            if u == UL and j == 2 * EARLY_G:
                                norm_sqrt(b, 0, 1)
                                for g in range(GROUPS // 2, GROUPS):
                                    copy_xT(b * LAYERS + 1, g, g % 2)
                                factors(b * LAYERS + 1, 1)
                                copy_sT(3 * b + 3, 4)
                                spread_s(b, u + 1)
                            pair = u * TP + j // 2
                            if j % 2 == 0 and not first(b * PAIRS + slot_before(pair) + 1):
                                act.wait_ge(s["pair_done"], b * PAIRS + slot_before(pair) + 1)
                            ins = act.activation(GL[:, SLOT[pair] * 2 + j % 2, :], sB[:, u % 2, :], ACT.Relu,
                                                 bias=sd[:, l, 1, h, j:j + 1])
                            if j % 2:
                                ins.then_inc(s["z_ready"], 1)
                            if j == 1 and ul + 1 < UL and u != UL:
                                spread_s(b, u + 1)
                            if u == UNITS - 1 and j == 6 and nxt is not None:
                                factors(nxt * LAYERS, 0)
                            if j == EVAC_AT and ul > 0:
                                evacuate(b, u - 1)
                            if j == EVAC_AT and u == 0 and prev is not None:
                                evacuate(prev, UNITS - 1)
                            if j == 13 and l == 1 and ul >= 2:
                                elu_exp(b, u - 2)
                            if j == 13 and u in (0, 1) and prev is not None:
                                elu_exp(prev, UNITS - 2 + u)
                            if j == 1 and u == 6:
                                norm_sqrt(b, 0, 0)
                            if j == 5 and u == UNITS - 1:
                                norm_sqrt(b, 1, 0)
                            if j == 5 and u == 3 and prev is not None:
                                norm_sqrt(prev, 1, 1)
                            if j == 14 and u == UNITS - 1:
                                normalise_rows(b, 0)
                            if j == 14 and u == 3 and prev is not None:
                                normalise_rows(prev, 1)
                            prep = prep_plan(u * T + j - ACT_LAG)
                            if prep is not None and (prep[0] == 1 or nxt is not None):
                                k = u * T + j - ACT_LAG
                                n = b * LAYERS + 1 if prep[0] else nxt * LAYERS
                                bk = JOB_BANK[k, *prep[1]][0]
                                if prep[1][0] == "T":
                                    copy_xT(n, prep[1][1], bk)
                                elif prep[1][0] == "S" and prep[0] == 0:
                                    copy_sT(3 * nxt + 1, bk)
                            if u == UNITS - 1 and j == 14 and nxt is not None:
                                spread_s(nxt, 0)

                work(0, range(0, EARLY), 1, None)
                if B > 1:
                    with act.Fori(0, B - 1) as b:
                        work(b, range(EARLY, UNITS), b + 1, None)
                        work(b + 1, range(0, EARLY), None, b)
                work(B - 1, range(EARLY, UNITS), None, None)
                evacuate(B - 1, UNITS - 1)
                elu_exp(B - 1, UNITS - 2)
                elu_exp(B - 1, UNITS - 1)
                norm_sqrt(B - 1, 1, 1)
                normalise_rows(B - 1, 1)
                store(B - 1, 1)
                act.wait_ge(s["out_dma"], 32 * B)

            @block.gpsimd
            def _(pool):
                pool.memset(idh[:, :], 0.0).then_inc(s["ident_ready"], 1)
                pool.memset(idf[:, :], 0.0).then_inc(s["ident_ready"], 1)
                pool.wait_ge(s["ident_ready"], 2)
                for m in (idh, idf):
                    pool.affine_select(out=m[:, :], in_=m[:, :], compare_op=ALU.not_equal, fill=1.0, base=0,
                                       pattern=[[-1, P]], channel_multiplier=1).then_inc(s["ident_ready"], 1)
                pool.memset(amat[:, :, :, :], 0.0).then_inc(s["ident_ready"], 1)
                pool.memset(bx[:, 1, :], 0.0).then_inc(s["ident_ready"], 1)
                pool.memset(F[:, :, :, C:CE], 1.0).then_inc(s["ident_ready"], 1)
                pool.memset(sd[:, :, :, :, :], 0.0).then_inc(s["ident_ready"], 1)

                steps = [0, 0]

                def link(ins, wait=True):
                    steps[1] += 1
                    ins.then_inc(s["pool_step"], 1)
                    if wait:
                        pool.wait_ge(s["pool_step"], steps[0] + steps[1])

                def split_features(n, l, h, parts=(0, 1)):
                    for q in parts:
                        f = F[:, :, h, :]
                        e = E[:, l, q, h, :].unsqueeze(2).to_broadcast([P, T, CE])
                        link(pool.tensor_tensor(V[:, h, :, 2 * q, :], f, e, ALU.mult), False)
                        link(pool.tensor_tensor(vt[:, :, :], f, e, ALU.mult))
                        last = pool.tensor_tensor(V[:, h, :, 2 * q + 1, :], vt[:, :, :], V[:, h, :, 2 * q, :],
                                                  ALU.subtract)
                        if q != parts[-1]:
                            link(last)
                    last.then_inc(s["v_ready"], 1)

                def c2_read(b, u):
                    pool.wait_ge(s["c2_ready"], b * UNITS + u + 1)

                def combine(b, u):
                    l, half, h = unit(u)
                    pool.wait_ge(s["evacuated"], PARTS * (b * UNITS + u + 1))
                    pool.tensor_tensor(vt[:, :, :], ev[:, :, 0, :], ev[:, :, 1, :], ALU.add).then_inc(s["ev_read"], 1)
                    pool.wait_ge(s["ev_read"], b * UNITS + u + 1)
                    v4 = vt[:, :, :].rearrange("p (q i) c -> p q i c", q=2)
                    link(pool.tensor_tensor(
                        v4, v4,
                        E[:, l, 2:4, h, half * TI:(half + 1) * TI].unsqueeze(3).to_broadcast([P, 2, TI, CE]),
                        ALU.mult))
                    pool.tensor_tensor(c2[:, :, :], vt[:, 0:TI, :], vt[:, TI:2 * TI, :], ALU.add)\
                        .then_inc(s["c2_ready"], 1)

                def normalise(b, u):
                    l, half, h = unit(u)
                    pool.wait_ge(s["recip_ready"], b * UNITS + u + 1)
                    if (l == 1 and u % UL > 0 or u == 0) and not first(b * UNITS + u):
                        pool.wait_ge(s["x_updated"], b * UNITS + u)
                    ins = pool.tensor_tensor(y[:, :, :], c2[:, :, 0:C],
                                             rc[:, :].unsqueeze(2).to_broadcast([P, TI, C]), ALU.mult)
                    if l == 1:
                        ins.then_inc(s["y_ready"], 1)
                    else:
                        link(ins)
                        if h == 0:
                            pool.wait_ge(x_dma[half], 16 * (b + 1))
                        xs = X[:, half * TI:(half + 1) * TI, h * C:(h + 1) * C]
                        pool.tensor_tensor(xs, xs, y[:, :, :], ALU.add).then_inc(s["x_updated"], 1)

                def elu_add(b, u):
                    _, half, h = unit(u)
                    pool.wait_ge(s["yexp_ready"], b * UL + u % UL + 1)
                    pool.sem_inc(s["pool_waited"], 1)
                    link(pool.tensor_scalar(y[:, :, :], y[:, :, :], 0.0, -1.0, ALU.max, ALU.add))
                    link(pool.tensor_tensor(y[:, :, :], y[:, :, :], ye[:, :, :], ALU.add))
                    xs = X[:, half * TI:(half + 1) * TI, h * C:(h + 1) * C]
                    pool.tensor_tensor(xs, xs, y[:, :, :], ALU.add).then_inc(s["x_updated"], 1)

                def maximum(n):
                    pool.wait_ge(s["pmax_ready"], n + 1)
                    pool.sem_inc(s["pool_waited"], 1)
                    pool.partition_all_reduce(dmx[:, :], pm[:, :], P, RMAX).then_inc(s["dmax_ready"], 1)

                def work(b, units, nxt, prev):
                    for u in units:
                        l, half, h = unit(u)
                        n = b * LAYERS + l
                        if u == UL:
                            maximum(n)
                            c2_read(b, u - 2)
                            pool.wait_ge(s["factors_ready"], n + 1)
                            split_features(n, 1, 0, (1,))
                        elif u > 0 or prev is not None:
                            bb, w = (b, u - 1) if u > 0 else (prev, UNITS - 1)
                            if u == 0:
                                pool.wait_ge(s["v_ready"], n * H + 1)
                            elif w % UL < H - 1:
                                pool.wait_ge(s["v_ready"], n * H + h + 1)
                            else:
                                c2_read(bb, w - 1)
                            combine(bb, w)
                        if half == 0 and h + 1 < H:
                            if u == UL or u == 0 and prev is None:
                                pool.wait_ge(s["v_ready"], n * H + 1)
                            else:
                                c2_read(bb, w)
                            split_features(n, l, h + 1)
                        if u == UNITS - 1 and nxt is not None:
                            c2_read(bb, w)
                            pool.wait_ge(s["factors_ready"], nxt * LAYERS + 1)
                            split_features(nxt * LAYERS, 0, 0)
                        if l == 1 and u % UL >= 2:
                            elu_add(b, u - 2)
                        if u in (0, 1) and prev is not None:
                            elu_add(prev, UNITS - 2 + u)
                        if u != UL and (u > 0 or prev is not None):
                            normalise(bb, w)
                        if u == UNITS - 2 and nxt is not None:
                            maximum(nxt * LAYERS)

                maximum(0)
                pool.wait_ge(s["factors_ready"], 1)
                split_features(0, 0, 0)
                work(0, range(0, EARLY), 1, None)
                SPLIT, HALF_SPLIT = 5, 2
                BEFORE = H * SPLIT + 2 * (EARLY - 1)
                PER_BATCH = (2 * H - 1) * SPLIT + HALF_SPLIT + (UNITS - 1) + (UL - 1) + 2 * UL
                assert steps == [0, BEFORE], steps
                if B > 1:
                    with pool.Fori(0, B - 1) as b:
                        steps[0], steps[1] = b * PER_BATCH + BEFORE, 0
                        work(b, range(EARLY, UNITS), b + 1, None)
                        work(b + 1, range(0, EARLY), None, b)
                        assert steps[1] == PER_BATCH, steps
                steps[0], steps[1] = (B - 1) * PER_BATCH + BEFORE, 0
                work(B - 1, range(EARLY, UNITS), None, None)
                c2_read(B - 1, UNITS - 2)
                combine(B - 1, UNITS - 1)
                elu_add(B - 1, UNITS - 2)
                normalise(B - 1, UNITS - 1)
                elu_add(B - 1, UNITS - 1)

            @block.vector
            def _(dve):
                dve.wait_ge(s["w_dma"], 16 * (3 * K + 1 + LAYERS * 2 * H))
                dve.tensor_copy(bwide, bcol[:, :].unsqueeze(2).to_broadcast([P, K, P])).then_inc(s["wt_copied"], 1)
                dve.wait_ge(s["wa_done"], 1)
                dve.wait_ge(s["wt_copied"], 3)
                dve.wait_ge(s["ident_ready"], 8)
                dve.tensor_copy(Wx[:, :, :, D:EX].rearrange("p l k e -> p (l k) e"),
                                bank[2][:, 0:LAYERS * K * 8].rearrange("p (a e) -> p a e", e=8)[:, :, 0:2 * H])
                dve.tensor_copy(bx[:, 0, D:EX], bank[2][:, 64:64 + 2 * H]).then_inc(s["const_ready"], 1)

                steps = [0, 0]

                def link(ins, wait=True):
                    steps[1] += 1
                    ins.then_inc(s["dve_step"], 1)
                    if wait:
                        dve.wait_ge(s["dve_step"], steps[0] + steps[1])

                def mask_copy(c, c_all, bk):
                    half, i, jh = c // CH, (c % CH) // 2, c % 2
                    it = half * TI + i
                    dve.wait_ge(s["mask_transposed"], c_all + 1)
                    dve.tensor_copy(M[:, jh * (T // 2):(jh + 1) * (T // 2), it * P:(it + 1) * P],
                                    bank[bk][:, :].bitcast(I16).rearrange("p (q n) -> p q n", n=P))\
                        .then_inc(s["mask_ready"], 1)

                def features(n, l, t, bk):
                    if t == 0:
                        if not first(n):
                            dve.wait_ge(s["v_ready"], n * H)
                    dve.wait_ge(s["projected"], n * T + t + 1)
                    pb = bank[bk]
                    dve.tensor_tensor(F[:, t, :, 0:C], pb[:, 0:D].rearrange("p (h c) -> p h c", h=H),
                                      bx[:, l, 0:D].rearrange("p (h c) -> p h c", h=H), ALU.add)
                    dve.tensor_tensor(sd[:, l, :, :, t], pb[:, D:EX].rearrange("p (q h) -> p q h", q=2),
                                      bx[:, l, D:EX].rearrange("p (q h) -> p q h", q=2), ALU.add)\
                        .then_inc(s["f_ready"], 1)

                def partial_max(n, l):
                    dve.wait_ge(s["f_ready"], n * T + T)
                    dve.tensor_reduce(pm[:, :], sd[:, l, 1, :, :], AX.X, ALU.max).then_inc(s["pmax_ready"], 1)

                def exponents(n, l):
                    dve.wait_ge(s["dmax_ready"], n + 1)
                    dm = dmx[:, :].unsqueeze(2).to_broadcast([P, H, T])
                    dve.tensor_tensor(Ein[:, 0, :, :], sd[:, l, 1, :, :], dm, ALU.subtract)
                    link(dve.tensor_tensor(uu[:, :, :], sd[:, l, 0, :, :], dm, ALU.add))
                    dve.tensor_scalar(Ein[:, 1, :, :], Ein[:, 0, :, :], SLOPE, None, ALU.mult)
                    dve.tensor_scalar(Ein[:, 2, :, :], uu[:, :, :], 1.0 - SLOPE, 0.0, ALU.mult, ALU.min)
                    dve.tensor_scalar(Ein[:, 3, :, :], uu[:, :, :], SLOPE - 1.0, 0.0, ALU.mult, ALU.min)\
                        .then_inc(s["expo_ready"], 1)

                def scale_factors(n, l):
                    dve.wait_ge(s["exp_ready"], n + 1)
                    dve.tensor_scalar(E[:, l, 0:2, :, :], E[:, l, 0:2, :, :], SCALE, None, ALU.mult)\
                        .then_inc(s["factors_ready"], 1)

                def reciprocal(b, u):
                    dve.wait_ge(s["c2_ready"], b * UNITS + u + 1)
                    dve.reciprocal(rc[:, :], c2[:, :, C]).then_inc(s["recip_ready"], 1)

                def stats(b, l, half, i):
                    if i == 0:
                        dve.wait_ge(s["x_updated"], b * UNITS + l * UL + half * H + H)
                    link(dve.bn_stats(st6[:, i, :], X[:, half * TI + i, :]), False)

                def variance(b):
                    dve.wait_ge(s["dve_step"], steps[0] + steps[1])
                    dve.sem_inc(s["dve_waited"], 1)
                    for i in range(TI):
                        last = dve.bn_aggr(mv[:, i, :], st6[:, i, :])
                    link(last)
                    dve.tensor_scalar(ve[:, :], mv[:, :, 1], EPS, None, ALU.add).then_inc(s["var_ready"], 1)

                def last_head(b, u):
                    l, half, h = unit(u)
                    for part, (b0_, b1_) in enumerate(EVAC):
                        dve.wait_ge(s["evacuated"], PARTS * (b * UNITS + u) + part + 1)
                        r = slice(b0_ * PER_BANK, min(b1_ * PER_BANK, 2 * TI))
                        ins = dve.tensor_tensor(ev[:, r, 0, :], ev[:, r, 0, :], ev[:, r, 1, :], ALU.add)
                        link(ins, part == len(EVAC) - 1)
                    e4 = ev[:, :, 0, :].rearrange("p (q i) c -> p q i c", q=2)
                    link(dve.tensor_tensor(
                        e4, e4,
                        E[:, l, 2:4, h, half * TI:(half + 1) * TI].unsqueeze(3).to_broadcast([P, 2, TI, CE]),
                        ALU.mult))
                    dve.wait_ge(s["x_updated"], b * UNITS + u)
                    dve.tensor_tensor(c2[:, :, :], ev[:, 0:TI, 0, :], ev[:, TI:2 * TI, 0, :], ALU.add)\
                        .then_inc(s["c2_ready"], 1)
                    reciprocal(b, u)
                    dve.sem_inc(s["ev_read"], 1)
                    dve.wait_ge(s["recip_ready"], b * UNITS + u + 1)
                    link(dve.tensor_tensor(y[:, :, :], c2[:, :, 0:C],
                                           rc[:, :].unsqueeze(2).to_broadcast([P, TI, C]), ALU.mult))
                    xs = X[:, half * TI:(half + 1) * TI, h * C:(h + 1) * C]
                    dve.tensor_tensor(xs, xs, y[:, :, :], ALU.add).then_inc(s["x_updated"], 1)

                def layer_norm(b, l, half):
                    dve.wait_ge(s["sqrt_ready"], b * 4 + l * 2 + half + 1)
                    link(dve.reciprocal(rs[:, :], sq[:, :]))
                    link(dve.tensor_tensor(nt[:, :], rs[:, :], rs[:, :], ALU.mult))
                    link(dve.tensor_tensor(nt[:, :], nt[:, :], ve[:, :], ALU.mult))
                    link(dve.tensor_scalar(nt[:, :], nt[:, :], -0.5, 1.5, ALU.mult, ALU.add))
                    link(dve.tensor_tensor(rs[:, :], rs[:, :], nt[:, :], ALU.mult))
                    if l == 1:
                        dve.scalar_tensor_tensor(nt[:, :], mv[:, :, 0], -1.0, rs[:, :], ALU.mult, ALU.mult)\
                            .then_inc(s["rs_ready"], 1)
                        return
                    for i in range(TI):
                        xi = X[:, half * TI + i, :]
                        last = dve.tensor_scalar(xi, xi, mv[:, i, 0:1], rs[:, i:i + 1], ALU.subtract, ALU.mult)
                        if (l, half) == (0, 1) and i % 2 == 1:
                            last.then_inc(s["tiles_normed"], 1)
                    if (l, half) != (0, 1):
                        last.then_inc(s["norm_ready"], 1)

                def first_head(n, b):
                    e = E[:, 1, 0, 0, :].unsqueeze(2).to_broadcast([P, T, CE])
                    dve.wait_ge(s["factors_ready"], n + 1)
                    dve.tensor_tensor(V[:, 0, :, 0, :], F[:, :, 0, :], e, ALU.mult)
                    dve.wait_ge(s["ev_read"], b * UNITS + UL)
                    link(dve.tensor_tensor(v0t, F[:, :, 0, :], e, ALU.mult))
                    dve.tensor_tensor(V[:, 0, :, 1, :], v0t, V[:, 0, :, 0, :], ALU.subtract).then_inc(s["v0_ready"], 1)

                for t in range(T):
                    features(0, 0, t, 2 + t % 2)
                partial_max(0, 0)
                exponents(0, 0)
                scale_factors(0, 0)
                for c in range(CH):
                    mask_copy(c, c, 6 + c % 2)

                def side_jobs(b, nxt, prev, u, j):
                    l, half, h = unit(u)
                    ul = u % UL
                    if j == 12 and ul > 0:
                        reciprocal(b, u - 1)
                    if j == 12 and u == 0 and prev is not None:
                        reciprocal(prev, UNITS - 1)
                    for at, (bb, ll, hh) in ((5, (b, 0, 0)), (UNITS - 2, (b, 1, 0)), (2, (prev, 1, 1))):
                        if u == at and bb is not None:
                            j0 = 7 if ll else 1
                            if j0 <= j < j0 + TI:
                                stats(bb, ll, hh, j - j0)
                            if j == j0 + TI:
                                variance(bb)
                        if u == at + 1 and j == (7 if ll else 1) and bb is not None:
                            layer_norm(bb, ll, hh)
                    for k in range(u * T + {1: -2, 3: -2, 5: 0}.get(j, j - 3),
                                   u * T + {1: -2, 3: 0, 5: 4}.get(j, j - 1)) if j % 2 else ():
                        c = MASK_AT.get((k // T, k % T))
                        if c is not None and (c >= CH or nxt is not None):
                            mask_copy(c, (b if c >= CH else nxt) * CHB + c, JOB_BANK[k, "M", c][0])
                        prep = prep_plan(k)
                        if prep is not None and prep[1][0] == "P" and (prep[0] == 1 or nxt is not None):
                            n = b * LAYERS + 1 if prep[0] else nxt * LAYERS
                            t = prep[1][1]
                            features(n, prep[0], t, JOB_BANK[k, "P", t][0])
                            if prep[0] == 0 and t == T - 1:
                                partial_max(n, 0)
                    if u == UNITS - 2 and j == 15 and nxt is not None:
                        exponents(nxt * LAYERS, 0)
                    if u == UNITS - 1 and j == 6 and nxt is not None:
                        scale_factors(nxt * LAYERS, 0)

                def operands(u, p):
                    slot, half = SLOT[u * TP + p], unit(u)[1]
                    return (GL[:, slot * 2:slot * 2 + 2, :],
                            M[:, 2 * p:2 * p + 2, half * HALF:(half + 1) * HALF])

                def upper(b, u, p):
                    g, m = operands(u, p)
                    dve.wait_ge(s["z_ready"], b * PAIRS + u * TP + p + 1)
                    dve.tensor_tensor(g, g, m, ALU.logical_and).then_inc(s["g_ready"], 1)

                def lower(b, u, p):
                    g, m = operands(u, p)
                    dve.wait_ge(s["g_used"], b * PAIRS + u * TP + p + 1)
                    dve.tensor_tensor(g, m, g, ALU.subtract).then_inc(s["l_ready"], 1)

                def work(b, units, nxt, prev):
                    for u in units:
                        l, half, h = unit(u)
                        if u == UL:
                            last_head(b, u - 1)
                            for i in range(TI):
                                stats(b, 0, 1, i)
                            variance(b)
                            upper(b, u, 0)
                            layer_norm(b, 0, 1)
                            n = b * LAYERS + 1
                            for t in range(T // 2, T):
                                features(n, 1, t, 2 + t % 2)
                                if t % 2 and 0 < t // 2 - T // 4 < EARLY_G:
                                    upper(b, u, t // 2 - T // 4)
                            partial_max(n, 1)
                            exponents(n, 1)
                            scale_factors(n, 1)
                            first_head(n, b)
                        if h == 0:
                            dve.wait_ge(s["mask_ready"], b * CHB + (CH if half == 0 else 2 * CH))
                        for jp in range(TP):
                            for step, (kind, p) in enumerate(PAIR_STEPS[jp]):
                                if kind == "L":
                                    lower(b, u, p)
                                elif u != UL or p >= EARLY_G:
                                    upper(b, u, p)
                                if step == 0:
                                    side_jobs(b, nxt, prev, u, 2 * jp)
                                if step == 1 or step == len(PAIR_STEPS[jp]) - 1 == 0:
                                    side_jobs(b, nxt, prev, u, 2 * jp + 1)

                work(0, range(0, EARLY), 1, None)
                BEFORE = 1
                PER_BATCH = LAYERS + 2 * LAYERS * (TI + 6) + 1 + PARTS + 2
                assert steps == [0, BEFORE], steps
                if B > 1:
                    with dve.Fori(0, B - 1) as b:
                        steps[0], steps[1] = b * PER_BATCH + BEFORE, 0
                        work(b, range(EARLY, UNITS), b + 1, None)
                        work(b + 1, range(0, EARLY), None, b)
                        assert steps[1] == PER_BATCH, steps
                steps[0], steps[1] = (B - 1) * PER_BATCH + BEFORE, 0
                work(B - 1, range(EARLY, UNITS), None, None)
                reciprocal(B - 1, UNITS - 1)
                for i in range(TI):
                    stats(B - 1, 1, 1, i)
                variance(B - 1)
                layer_norm(B - 1, 1, 1)


_INS = ["x", "adj", "L0_gnn_W", "L0_gnn_b", "L0_gnn_a", "L1_gnn_W", "L1_gnn_a_src", "L1_gnn_a_dst"]


def kernel(**inputs):
    import numpy as _np
    import concourse.bacc as _bacc
    from concourse import mybir as _mybir
    from concourse.bass_utils import run_bass_kernel_spmd as _run

    nc = _bacc.Bacc("TRN2", target_bir_lowering=False, num_devices=1)
    arrays, args = {}, []
    for name in _INS:
        a = _np.ascontiguousarray(inputs[name])
        arrays[f"in_{name}_dram"] = a
        args.append(nc.dram_tensor(f"in_{name}_dram", a.shape, _mybir.dt.from_np(a.dtype), kind="ExternalInput").ap())
    out = nc.dram_tensor("out_0_dram", inputs["x"].shape, _mybir.dt.float32, kind="ExternalOutput").ap()
    gat_kernel(nc, *args, out)
    r = _run(nc, [arrays], core_ids=[0])
    return r.results[0]["out_0_dram"]
```
